# Optimizing a Trainium2 kernel written in Bass

```python
import numpy as np
import jax
import jax.numpy as jnp

def _softmax(x, axis=-1):
    return jax.nn.softmax(x, axis=axis)

def _gelu(x):
    return jax.nn.gelu(x, approximate=True)

def _silu(x):
    return jax.nn.silu(x)

def _sigmoid(x):
    return jax.nn.sigmoid(x)

def _layernorm(x, axis=-1, eps=1e-05):
    m = jnp.mean(x, axis=axis, keepdims=True)
    v = jnp.var(x, axis=axis, keepdims=True)
    return (x - m) / jnp.sqrt(v + eps)

def _scatter_add(tgt, idx, src, axis=0):
    return tgt.at[idx].add(src)

def _segment_sum(src, seg, n):
    return jax.ops.segment_sum(src, seg, n)
kernel_name = 'mk_conv_seq_d2_conv_nchw16_r2_356d16'

def setup_inputs(seed: int=0):
    np.random.seed(seed)
    _w = jnp.asarray

    def _rec_inputs():
        import jax
        import jax.numpy as jnp
        _gk = jax.random.key(seed)
        x = -7.109e-05 + 0.9999 * jax.random.normal(jax.random.fold_in(_gk, 1), (1, 16, 1024, 1024), jnp.float32)
        return x
    x = _rec_inputs()

    def _L0_conv_setup():
        import jax, jax.numpy as jnp
        import numpy as np
        EPS = 1e-06
        key = jax.random.key(seed)
        k0, k1, k2 = jax.random.split(key, 3)
        B, H, S, MW = (1, 16, 1024, 32)
        x = jax.random.normal(k0, (B, H, S, S), dtype=jnp.float32)
        W1 = jax.random.normal(k1, (1, MW), dtype=jnp.float32)
        b1 = jnp.zeros((MW,), dtype=jnp.float32)
        W2 = jax.random.normal(k2, (MW, H), dtype=jnp.float32) * (1.0 / np.sqrt(MW))
        b2 = jnp.zeros((H,), dtype=jnp.float32)
        c = jnp.float32(0.1)
        L_multiplier = jnp.float32(1.0)
        init_L = jnp.float32(512.0)
        return {'x': x, 'W1': W1, 'b1': b1, 'W2': W2, 'b2': b2, 'c': c, 'L_multiplier': L_multiplier, 'init_L': init_L}
    _L0_conv_all = _L0_conv_setup()
    _L0_conv_in = {k: v for k, v in _L0_conv_all.items() if k in ('W1', 'b1', 'W2', 'b2', 'c', 'L_multiplier', 'init_L')}
    del _L0_conv_all

    def _L1_conv_setup():
        import jax, jax.numpy as jnp
        import numpy as np
        B, N, T, S = (1, 16, 1024, 1024)
        G, I = (1, 2)
        M = N // G
        key = jax.random.key(seed)
        ks = jax.random.split(key, 8)
        return {'inputs': jax.random.normal(ks[0], (B, N, T, S), dtype=jnp.float32), 'qw1': jax.random.normal(ks[1], (B, T, G, I, M), dtype=jnp.float32) * 0.05, 'qw2': jax.random.normal(ks[2], (B, T, G, I, M), dtype=jnp.float32) * 0.05, 'kw1': jax.random.normal(ks[3], (B, S, G, I, M), dtype=jnp.float32) * 0.05, 'kw2': jax.random.normal(ks[4], (B, S, G, I, M), dtype=jnp.float32) * 0.05, 'qdd': jax.random.normal(ks[5], (B, T, G, M), dtype=jnp.float32) * 0.05, 'kdd': jax.random.normal(ks[6], (B, S, G, M), dtype=jnp.float32) * 0.05, 'w': jax.random.normal(ks[7], (G, M, M), dtype=jnp.float32) * 0.02}
    _L1_conv_all = _L1_conv_setup()
    _L1_conv_in = {k: v for k, v in _L1_conv_all.items() if k in ('qw1', 'qw2', 'kw1', 'kw2', 'qdd', 'kdd', 'w')}
    del _L1_conv_all
    return {'x': x, 'L0_conv_W1': _L0_conv_in['W1'], 'L0_conv_b1': _L0_conv_in['b1'], 'L0_conv_W2': _L0_conv_in['W2'], 'L0_conv_b2': _L0_conv_in['b2'], 'L0_conv_c': _L0_conv_in['c'], 'L0_conv_L_multiplier': _L0_conv_in['L_multiplier'], 'L0_conv_init_L': _L0_conv_in['init_L'], 'L1_conv_qw1': _L1_conv_in['qw1'], 'L1_conv_qw2': _L1_conv_in['qw2'], 'L1_conv_kw1': _L1_conv_in['kw1'], 'L1_conv_kw2': _L1_conv_in['kw2'], 'L1_conv_qdd': _L1_conv_in['qdd'], 'L1_conv_kdd': _L1_conv_in['kdd'], 'L1_conv_w': _L1_conv_in['w']}

def reference(x, L0_conv_W1, L0_conv_b1, L0_conv_W2, L0_conv_b2, L0_conv_c, L0_conv_L_multiplier, L0_conv_init_L, L1_conv_qw1, L1_conv_qw2, L1_conv_kw1, L1_conv_kw2, L1_conv_qdd, L1_conv_kdd, L1_conv_w):
    import jax
    import jax.numpy as jnp

    def _L0_conv_ref(x, W1, b1, W2, b2, c, L_multiplier, init_L):
        import jax, jax.numpy as jnp
        import numpy as np
        EPS = 1e-06
        S = x.shape[-1]
        idx = jnp.arange(S)
        rel = jnp.tril(idx[:, None] - idx[None, :]).astype(jnp.float32)
        threshold = jnp.abs(L_multiplier * init_L)
        pos = jnp.maximum(rel.max(axis=-1), threshold)[:, None]
        nd = jnp.log(jnp.abs(c * rel) + 1.0) / (jnp.log(jnp.abs(c * pos) + 1.0) + EPS)
        nd = nd.astype(x.dtype)
        h = jax.nn.relu(nd[..., None] * W1[0] + b1)
        bias = jnp.einsum('qkm,mh->qkh', h, W2) + b2
        return x + bias.transpose(2, 0, 1)[None]

    def _L1_conv_ref(inputs, qw1, qw2, kw1, kw2, qdd, kdd, w):
        import jax, jax.numpy as jnp
        import numpy as np
        B, N, T, S = (1, 16, 1024, 1024)
        G, I = (1, 2)
        M = N // G
        b, n, t, s = inputs.shape
        g, m = (w.shape[0], w.shape[1])
        x = inputs.reshape(b, g, m, t, s)
        wi = w + jnp.eye(m, dtype=w.dtype)
        ret = jnp.einsum('BGMTS,GMN->BGNTS', x, wi)
        hq = jnp.einsum('BGMTS,BTGIM->BGITS', x, qw1)
        ret = ret + jnp.einsum('BGITS,BTGIM->BGMTS', hq, qw2)
        hk = jnp.einsum('BGMTS,BSGIM->BGITS', x, kw1)
        ret = ret + jnp.einsum('BGITS,BSGIM->BGMTS', hk, kw2)
        ret = ret + jnp.einsum('BGMTS,BTGM->BGMTS', x, qdd)
        ret = ret + jnp.einsum('BGMTS,BSGM->BGMTS', x, kdd)
        return ret.reshape(b, n, t, s)

    def _gn(v, G=8, eps=1e-05):
        B_, C_, H_, W_ = v.shape
        g = v.reshape(B_, G, C_ // G, H_, W_)
        m = jnp.mean(g, axis=(2, 3, 4), keepdims=True)
        s = jnp.var(g, axis=(2, 3, 4), keepdims=True)
        return ((g - m) / jnp.sqrt(s + eps)).reshape(v.shape)

    def _ln_c(v, eps=1e-06):
        m = jnp.mean(v, axis=1, keepdims=True)
        s = jnp.var(v, axis=1, keepdims=True)
        return (v - m) / jnp.sqrt(s + eps)

    def _ln_t(v, eps=1e-05):
        m = jnp.mean(v, axis=-1, keepdims=True)
        s = jnp.var(v, axis=-1, keepdims=True)
        return (v - m) / jnp.sqrt(s + eps)

    def _to_tokens(v):
        B_, C_, H_, W_ = v.shape
        return v.reshape(B_, C_, H_ * W_).transpose(0, 2, 1)

    def _from_tokens(t, like):
        B_, C_, H_, W_ = like.shape
        return t.transpose(0, 2, 1).reshape(B_, C_, H_, W_)
    x = _L0_conv_ref(x, L0_conv_W1, L0_conv_b1, L0_conv_W2, L0_conv_b2, L0_conv_c, L0_conv_L_multiplier, L0_conv_init_L)
    x = _L1_conv_ref(x, L1_conv_qw1, L1_conv_qw2, L1_conv_kw1, L1_conv_kw2, L1_conv_qdd, L1_conv_kdd, L1_conv_w)
    return x

_drawn_inputs = setup_inputs


def setup_inputs(seed=0):
    import zlib

    import numpy as np

    out = dict(_drawn_inputs(seed))
    spreads = {'L0_conv_b1': (0.0, 0.1), 'L0_conv_b2': (0.0, 0.1)}
    factors = {'L1_conv_qw1': 4.033, 'L1_conv_qw2': 4.011, 'L1_conv_kw1': 3.98, 'L1_conv_kw2': 3.996}
    for name, (base, spread) in spreads.items():
        noise = np.random.default_rng([zlib.crc32(name.encode()), seed]).standard_normal(out[name].shape)
        drawn = base * np.exp(spread * noise) if base else spread * noise
        out[name] = jnp.asarray(drawn.astype(out[name].dtype))
    for name, factor in factors.items():
        out[name] = (out[name] * factor).astype(out[name].dtype)
    return out
```

```python
import concourse.bass as bass
from concourse import mybir

F32 = mybir.dt.float32
ALU = mybir.AluOpType
ACT = mybir.ActivationFunctionType

P = 128
H = 16
S = 1024
BLOCKS = P // H
W = S // BLOCKS
REGIONS = S // W
HID = 32
SLOTS = P // HID
ROWS = 8
COLS = ROWS * W
BANK = 512
CHUNK = 32
CHUNKS = W // CHUNK
PAIRS = CHUNK // (2 * ROWS)
TILES = W // ROWS
HALF = REGIONS // 2
SETUP_TILES = 4
TABLE = S + W - 1
DMA = 16
PER_CHUNK = BLOCKS * DMA
EPS = 1e-6


def build(nc, x, W1, b1, W2, b2, c, L_mult, init_L, qw1, qw2, kw1, kw2, qdd, kdd, w, out):
    a_mats = nc.dram_tensor("a_mats", (REGIONS, CHUNKS, H, H * CHUNK), F32, kind="Internal").ap()
    b_mats = nc.dram_tensor("b_mats", (BLOCKS, CHUNKS, H, H * CHUNK), F32, kind="Internal").ap()

    from contextlib import ExitStack
    with ExitStack() as ctx:
        def sb(name, shape):
            return ctx.enter_context(nc.sbuf_tensor(name, shape, F32))

        def sem(name):
            return ctx.enter_context(nc.semaphore(name))

        y = sb("y", [P, W, W])
        mixed = sb("mixed", [P, W, W])
        mats = sb("mats", [P, 2, P, CHUNK])
        nd = sb("nd", [P, 2, COLS])
        hidden = sb("hidden", [P, 2, COLS])
        log_table = sb("log_table", [P, TABLE])
        row_scale = sb("row_scale", [P, S])
        w2_blocks = sb("w2_blocks", [P, 2, P])
        ident = sb("ident", [P, P])
        w1_col = sb("w1_col", [P, 1])
        b1_col = sb("b1_col", [P, 1])
        b2_col = sb("b2_col", [P, 2])
        relu_b1 = sb("relu_b1", [P, 1])
        c_col = sb("c_col", [P, 1])
        thr_col = sb("thr_col", [P, 3])

        spare = mixed[:].rearrange("p t s -> p (t s)")
        comp = {"a": spare[:, 0:2048], "b": spare[:, 2048:4096]}
        term = spare[:, 4096:6144]
        turned = {"a": spare[:, 6144:8192], "b": spare[:, 8192:10240]}
        first = {"a": spare[:, 10240:10496], "b": spare[:, 10496:10752]}
        second = {"a": spare[:, 10752:11008], "b": spare[:, 11008:11264]}
        diag = {"a": spare[:, 11264:11392], "b": spare[:, 11392:11520]}
        w_eye = spare[:, 11520:11776]

        main = ctx.enter_context(nc.psum_tensor("main", [P, 2, COLS], F32))
        bias = ctx.enter_context(nc.psum_tensor("bias", [P, 2, COLS], F32))

        weights_in = {"a": sem("weights_in_a"), "b": sem("weights_in_b")}
        consts_in = sem("consts_in")
        w2_in = sem("w2_in")
        w2_zeroed = sem("w2_zeroed")
        mats_zeroed = sem("mats_zeroed")
        indices_made = sem("indices_made")
        ident_made = sem("ident_made")
        dve_step = sem("dve_step")
        logs_wanted = sem("logs_wanted")
        logs_made = sem("logs_made")
        tables_made = sem("tables_made")
        comp_made = sem("comp_made")
        b_mats_out = sem("b_mats_out")
        a_mats_out = sem("a_mats_out")
        relu_b1_made = sem("relu_b1_made")
        const_bias_made = sem("const_bias_made")
        const_bias_read = sem("const_bias_read")

        x_in = [sem(f"x_in{i}") for i in range(CHUNKS)]
        mats_in = [sem(f"mats_in{i}") for i in range(2)]
        nd_ready = sem("nd_ready")
        hidden_ready = sem("hidden_ready")
        hidden_used = sem("hidden_used")
        y_ready = sem("y_ready")
        main_ready = sem("main_ready")
        main_taken = sem("main_taken")
        out_done = sem("out_done")

        def region_tiles(k, T):
            return k * TILES + T

        def hidden_index(k, T, g, groups):
            if groups == 1:
                return k * TILES + T
            return (k - HALF) * (2 * TILES) + (HALF * TILES + g) + T * 2

        def b_tile(k, T):
            return k * (2 * TILES) + (SETUP_TILES + T)

        def a_tile(k, T):
            return k * (2 * TILES) + (SETUP_TILES + TILES + T)

        def b_chunk(k, cc):
            return k * (2 * CHUNKS) + cc

        def a_chunk(k, cc):
            return k * (2 * CHUNKS) + (CHUNKS + cc)

        def tiles_before(chunk):
            return chunk * (2 * PAIRS) + SETUP_TILES

        def ring_use(chunk_of, k, cc):
            return k * CHUNKS + (chunk_of(0, cc) // 2 + 1)

        def wait(eng, semaphore, count):
            if not (isinstance(count, int) and count <= 0):
                eng.wait_ge(semaphore, count)

        def each_pair(eng, body, unrolled=False):
            if unrolled:
                for p in range(PAIRS):
                    body(p)
            else:
                with eng.Fori(0, PAIRS) as p:
                    body(p)

        def stages(eng, stage):
            stage(0, mix_a=False, groups=1)
            with eng.Fori(1, HALF) as k:
                stage(k, mix_a=True, groups=1)
            with eng.Fori(HALF, REGIONS) as k:
                stage(k, mix_a=True, groups=2)
            stage(REGIONS, mix_a=True, groups=0)

        def rows(tile, first_row, n):
            return tile[:, bass.ds(first_row, n), :].rearrange("p t s -> p (t s)")

        def slot_of(ring, slot):
            return ring[:, slot, :]

        block = ctx.enter_context(nc.Block())

        @block.sync
        def _(sp):
            for part, v1, v2, vd in (("b", kw1, kw2, kdd), ("a", qw1, qw2, qdd)):
                for dst, src in ((first[part], v1), (second[part], v2)):
                    sp.dma_start(dst.rearrange("p (b i) -> p b i", b=BLOCKS),
                                 src.rearrange("o (b p) g i m -> p (o b) (g i m)", p=P)).then_inc(weights_in[part], DMA)
                sp.dma_start(diag[part].rearrange("p (b m) -> p b m", b=BLOCKS),
                             vd.rearrange("o (b p) g m -> p (o b) (g m)", p=P)).then_inc(weights_in[part], DMA)
                if part == "b":
                    sp.dma_start(c_col[:], c.partition_broadcast(P)).then_inc(consts_in, DMA)
                    sp.dma_start(thr_col[:, 0:1], L_mult.partition_broadcast(P)).then_inc(consts_in, DMA)
                    sp.dma_start(thr_col[:, 1:2], init_L.partition_broadcast(P)).then_inc(consts_in, DMA)
                    for q in range(SLOTS):
                        part_q = slice(HID * q, HID * (q + 1))
                        sp.dma_start(w1_col[part_q, :], W1.rearrange("o m -> m o")).then_inc(consts_in, DMA)
                        sp.dma_start(b1_col[part_q, :], b1.rearrange("(m o) -> m o", o=1)).then_inc(consts_in, DMA)
                    for b in range(BLOCKS):
                        sp.dma_start(b2_col[H * b:H * (b + 1), 0:1], b2.rearrange("(h o) -> h o", o=1)).then_inc(consts_in, DMA)
                    sp.wait_ge(w2_zeroed, 1)
                    for g in range(2):
                        for q in range(SLOTS):
                            col = H * (SLOTS * g + q)
                            sp.dma_start(w2_blocks[HID * q:HID * (q + 1), g, col:col + H], W2).then_inc(w2_in, DMA)
                else:
                    sp.dma_start(w_eye, w.rearrange("g m n -> g (m n)").partition_broadcast(P)).then_inc(weights_in["a"], DMA)

            def load_x(k, cc):
                for b in range(BLOCKS):
                    sp.dma_start(y[H * b:H * (b + 1), cc * CHUNK:(cc + 1) * CHUNK, :],
                                 x[0, :, bass.ds(k * W + cc * CHUNK, CHUNK), b * W:(b + 1) * W]).then_inc(x_in[cc], DMA)

            def store(k, cc):
                sp.wait_ge(main_taken, tiles_before(a_chunk(k, cc) + 1))
                for b in range(BLOCKS):
                    sp.dma_start(out[0, :, bass.ds(k * W + cc * CHUNK, CHUNK), b * W:(b + 1) * W],
                                 mixed[H * b:H * (b + 1), cc * CHUNK:(cc + 1) * CHUNK, :]).then_inc(out_done, DMA)

            def load_mats(chunk_of, k, cc):
                sp.wait_ge(main_ready, tiles_before(chunk_of(k, cc) - 1))
                slot = cc % 2
                for b in range(BLOCKS):
                    dst = mats[H * b:H * (b + 1), slot, H * b:H * (b + 1), :].rearrange("p n e -> p (n e)")
                    if chunk_of is b_chunk:
                        src = b_mats[b, cc]
                    else:
                        src = a_mats[bass.ds(k, 1), cc].rearrange("o m f -> (o m) f")
                    sp.dma_start(dst, src).then_inc(mats_in[slot], DMA)

            def stage(k, mix_a, groups):
                if mix_a:
                    load_mats(a_chunk, k - 1, 0)
                    load_mats(a_chunk, k - 1, 1)
                else:
                    for cc in range(CHUNKS):
                        load_x(k, cc)
                    for part, mat, done in (("b", b_mats, b_mats_out), ("a", a_mats, a_mats_out)):
                        for half in range(2):
                            sp.wait_ge(main_taken, 2 * (part == "a") + half + 1)
                            src = turned[part][:, half * COLS:(half + 1) * COLS].rearrange("p (j e) -> p j e", e=CHUNK)
                            dst = mat[:, :, half * (H // 2):(half + 1) * (H // 2), :].rearrange(
                                "b j m (n e) -> (m n) (b j) e", e=CHUNK)
                            sp.dma_start(dst, src).then_inc(done, DMA)
                    sp.wait_ge(b_mats_out, 2 * DMA)
                    sp.wait_ge(mats_zeroed, 1)
                for cc in range(CHUNKS):
                    if mix_a:
                        if groups:
                            sp.wait_ge(main_ready, tiles_before(a_chunk(k - 1, cc) + 1))
                            load_x(k, cc)
                        if cc + 2 < CHUNKS:
                            load_mats(a_chunk, k - 1, cc + 2)
                        elif groups:
                            load_mats(b_chunk, k, cc + 2 - CHUNKS)
                        store(k - 1, cc)
                    elif cc < 2:
                        load_mats(b_chunk, k, cc)
                if groups:
                    load_mats(b_chunk, k, 2)
                    load_mats(b_chunk, k, 3)
                if not mix_a:
                    sp.wait_ge(a_mats_out, 2 * DMA)

            stages(sp, stage)
            sp.wait_ge(out_done, REGIONS * CHUNKS * PER_CHUNK)

        @block.gpsimd
        def _(pool):
            for q in range(SLOTS):
                nc.gpsimd.iota(log_table[HID * q:HID * (q + 1), :], pattern=[[1, TABLE]], base=-(W - 1) - W * q,
                               channel_multiplier=0, allow_small_or_imprecise_dtypes=True).then_inc(indices_made, 1)
            pool.wait_ge(indices_made, SLOTS)
            nc.gpsimd.iota(row_scale[:], pattern=[[1, S]], base=0, channel_multiplier=0,
                           allow_small_or_imprecise_dtypes=True).then_inc(indices_made, 1)
            pool.wait_ge(indices_made, SLOTS + 1)
            nc.gpsimd.memset(ident[:], 0.0).then_inc(ident_made, 1)
            pool.wait_ge(ident_made, 1)
            nc.gpsimd.affine_select(out=ident[:], in_=ident[:], compare_op=ALU.not_equal, fill=1.0, base=0,
                                    pattern=[[-1, P]], channel_multiplier=1).then_inc(ident_made, 1)
            pool.wait_ge(ident_made, 2)
            nc.gpsimd.memset(mats[:], 0.0).then_inc(mats_zeroed, 1)
            pool.wait_ge(mats_zeroed, 1)
            pool.wait_ge(tables_made, 1)

            def stage(k, mix_a, groups):
                if not groups:
                    return
                for cc in range(CHUNKS):
                    def pair(p):
                        for half in range(2):
                            T = p * 2 + (2 * PAIRS * cc + half)
                            for g in range(groups):
                                n = hidden_index(k, T, g, groups)
                                slot = (half if groups == 1 else g)
                                wait(pool, hidden_ready, n - 1)
                                t0 = k * W + T * ROWS
                                logs = log_table[:, bass.ds(t0 - SLOTS * W * g, ROWS)]
                                scales = row_scale[:, bass.ds(t0, ROWS)]
                                pool.tensor_tensor(
                                    slot_of(nd, slot).rearrange("p (j s) -> p j s", j=ROWS),
                                    bass.AP(logs.tensor, logs.offset, [list(logs.ap[0]), [1, ROWS], [1, W]]),
                                    bass.AP(scales.tensor, scales.offset, [list(scales.ap[0]), [1, ROWS], [0, W]]),
                                    ALU.mult).then_inc(nd_ready, 1)
                    each_pair(pool, pair, unrolled=(not mix_a and cc == 0))

            stages(pool, stage)

        @block.scalar
        def _(act):
            act.wait_ge(logs_wanted, 1)
            nc.scalar.activation(log_table[:], log_table[:], ACT.Ln, bias=1.0).then_inc(logs_made, 1)
            act.wait_ge(logs_wanted, 2)
            nc.scalar.activation(row_scale[:], row_scale[:], ACT.Ln, bias=1.0).then_inc(logs_made, 1)
            act.wait_ge(consts_in, 19 * DMA)
            nc.scalar.activation(relu_b1[:], b1_col[:], ACT.Relu).then_inc(relu_b1_made, 1)

            def stage(k, mix_a, groups):
                if not groups:
                    return
                for cc in range(CHUNKS):
                    def pair(p):
                        for half in range(2):
                            T = p * 2 + (2 * PAIRS * cc + half)
                            for g in range(groups):
                                n = hidden_index(k, T, g, groups)
                                slot = (half if groups == 1 else g)
                                act.wait_ge(nd_ready, n + 1)
                                wait(act, hidden_used, n - 1)
                                nc.scalar.activation(slot_of(hidden, slot), slot_of(nd, slot), ACT.Relu,
                                                     bias=b1_col[:, 0:1], scale=w1_col[:, 0:1]).then_inc(hidden_ready, 1)
                    each_pair(act, pair, unrolled=(not mix_a and cc == 0))
                if mix_a:
                    act.wait_ge(out_done, k * (CHUNKS * PER_CHUNK))
                else:
                    act.wait_ge(b_mats_out, 2 * DMA)
                    act.wait_ge(a_mats_out, 2 * DMA)
                with act.Fori(0, TILES // 2) as p:
                    for half in range(2):
                        T = p * 2 + half
                        act.wait_ge(main_ready, b_tile(k, T) + 1)
                        nc.scalar.activation(mixed[:, :, bass.ds(T * ROWS, ROWS)],
                                             slot_of(main, half).rearrange("p (s t) -> p t s", s=ROWS),
                                             ACT.Copy).then_inc(main_taken, 1)

            stages(act, stage)

        @block.vector
        def _(dve):
            steps = [0]

            def step(instruction):
                steps[0] += 1
                instruction.then_inc(dve_step, 1)
                dve.wait_ge(dve_step, steps[0])

            def absolute(ap):
                return dve.scalar_tensor_tensor(out=ap, in0=ap, scalar=-1.0, in1=ap, op0=ALU.mult, op1=ALU.max)

            dve.memset(w2_blocks[:], 0.0).then_inc(w2_zeroed, 1)
            dve.wait_ge(consts_in, 19 * DMA)
            dve.wait_ge(indices_made, SLOTS + 1)
            step(dve.tensor_scalar(log_table[:], log_table[:], 0.0, c_col[:, 0:1], ALU.max, ALU.mult))
            absolute(log_table[:]).then_inc(logs_wanted, 1)
            step(dve.tensor_tensor(thr_col[:, 2:3], thr_col[:, 0:1], thr_col[:, 1:2], ALU.mult))
            step(absolute(thr_col[:, 2:3]))
            step(dve.tensor_scalar(row_scale[:], row_scale[:], thr_col[:, 2:3], c_col[:, 0:1], ALU.max, ALU.mult))
            absolute(row_scale[:]).then_inc(logs_wanted, 1)

            def square(ap):
                return ap.rearrange("p (b m n) -> p b m n", b=BLOCKS, m=H)

            def rank_one(part, i, dst):
                shape = [P, BLOCKS, H, H]
                u = first[part].rearrange("p (b i m) -> p b i m", b=BLOCKS, i=2)[:, :, i, :]
                v = second[part].rearrange("p (b i m) -> p b i m", b=BLOCKS, i=2)[:, :, i, :]
                return dve.tensor_tensor(square(dst), u.unsqueeze(3).to_broadcast(shape),
                                         v.unsqueeze(2).to_broadcast(shape), ALU.mult)

            def diagonal(ap, blocks):
                return bass.AP(ap.tensor, ap.offset, [list(ap.ap[0]), [H * H, blocks], [H + 1, H]])

            def compact(part):
                dve.wait_ge(weights_in[part], DMA * (3 + (part == "a")))
                if part == "a":
                    eye = diagonal(w_eye, 1)
                    step(dve.tensor_scalar(eye, eye, 1.0, None, ALU.add))
                rank_one(part, 0, comp[part])
                step(rank_one(part, 1, term))
                step(dve.tensor_tensor(comp[part], comp[part], term, ALU.add))
                if part == "a":
                    whole = comp[part].rearrange("p (b f) -> p b f", b=BLOCKS)
                    step(dve.tensor_tensor(whole, whole, w_eye.unsqueeze(1).to_broadcast([P, BLOCKS, H * H]), ALU.add))
                on = diagonal(comp[part], BLOCKS)
                dve.tensor_tensor(on, on, diag[part].rearrange("p (b m) -> p b m", b=BLOCKS), ALU.add)\
                   .then_inc(comp_made, 1)

            def turn_out(part, half):
                n = 2 * (part == "a") + half
                dve.wait_ge(main_ready, n + 1)
                dve.tensor_copy(turned[part][:, half * COLS:(half + 1) * COLS], slot_of(main, half))\
                   .then_inc(main_taken, 1)

            compact("b")
            dve.wait_ge(logs_made, 2)
            step(dve.tensor_scalar(row_scale[:], row_scale[:], EPS, None, ALU.add))
            dve.reciprocal(row_scale[:], row_scale[:]).then_inc(tables_made, 1)
            turn_out("b", 0)
            turn_out("b", 1)
            compact("a")
            turn_out("a", 0)
            turn_out("a", 1)
            step(dve.tensor_copy(b2_col[:, 1:2], b2_col[:, 0:1]))
            dve.wait_ge(const_bias_made, 1)
            dve.tensor_tensor(b2_col[P // 2:, 1:2], b2_col[P // 2:, 0:1], bias[P // 2:, 1, 0:1], ALU.add)\
               .then_inc(const_bias_read, 1)
            dve.wait_ge(const_bias_read, 1)

            def finish_tile(k, T, half):
                dve.wait_ge(main_taken, b_tile(k, TILES - 1) + 1)
                dve.wait_ge(main_ready, a_tile(k, T) + 1)
                dve.tensor_tensor(rows(mixed, T * ROWS, ROWS), slot_of(main, half), rows(mixed, T * ROWS, ROWS),
                                  ALU.add).then_inc(main_taken, 1)

            def add_bias(k, cc, T, half, groups):
                dve.wait_ge(x_in[cc], k * PER_CHUNK + PER_CHUNK)
                dve.wait_ge(hidden_used, hidden_index(k, T, groups - 1, groups) + 1)
                falling = bass.AP(bias, half * COLS + W - 1, [[2 * COLS, P], [W, ROWS], [-1, W]])
                y_rows = y[:, bass.ds(T * ROWS, ROWS), :]
                dve.scalar_tensor_tensor(out=y_rows, in0=falling, scalar=b2_col[:, 2 - groups:3 - groups], in1=y_rows,
                                         op0=ALU.add, op1=ALU.add).then_inc(y_ready, 1)

            def stage(k, mix_a, groups):
                for cc in range(CHUNKS + 1):
                    a_here = mix_a and cc < CHUNKS
                    bias_here = groups and cc > 0
                    if not (a_here or bias_here):
                        continue

                    def pair(p):
                        for half in range(2):
                            if a_here:
                                finish_tile(k - 1, p * 2 + (2 * PAIRS * cc + half), half)
                            if bias_here:
                                add_bias(k, cc - 1, p * 2 + (2 * PAIRS * (cc - 1) + half), half, groups)
                    each_pair(dve, pair)

            stages(dve, stage)

        @block.tensor
        def _(pe):
            pe.wait_ge(ident_made, 2)
            for n, (part, half) in enumerate((part, half) for part in "ba" for half in range(2)):
                pe.wait_ge(comp_made, 1 + (part == "a"))
                wait(pe, main_taken, n - 1)
                for b in range(BLOCKS):
                    at = (2 * b + half) * P
                    mm = pe.transpose(main[:, half, b * P:(b + 1) * P], comp[part][:, at:at + P], ident[:])
                mm.then_inc(main_ready, 1)
            pe.wait_ge(w2_in, 2 * SLOTS * DMA)
            pe.wait_ge(relu_b1_made, 1)
            for g in range(2):
                mm = pe.matmul(bias[:, 1, 0:1], w2_blocks[:, g, :], relu_b1[:, 0:1], start=(g == 0), stop=(g == 1))
            mm.then_inc(const_bias_made, 1)
            pe.wait_ge(const_bias_read, 1)

            def a_rows(k, cc, T, half, first_row):
                pe.wait_ge(main_taken, a_tile(k, T) - 1)
                for j in range(ROWS):
                    mm = pe.matmul(main[:, half, j * W:(j + 1) * W],
                                   mats[:, cc % 2, :, first_row + j], y[:, T * ROWS + j, :], start=True, stop=True)
                mm.then_inc(main_ready, 1)

            def bias_tile(k, T, half, groups):
                wait(pe, y_ready, region_tiles(k, T) - 1)
                for g in range(groups):
                    pe.wait_ge(hidden_ready, hidden_index(k, T, g, groups) + 1)
                    slot = (half if groups == 1 else g)
                    for at in range(0, COLS, BANK):
                        mm = pe.matmul(bias[:, half, at:at + BANK], w2_blocks[:, g, :],
                                       slot_of(hidden, slot)[:, at:at + BANK], start=(g == 0), stop=(g == groups - 1))
                    mm.then_inc(hidden_used, 1)

            def stage(k, mix_a, groups):
                for cc in range(CHUNKS + 1):
                    a_here = mix_a and cc < CHUNKS
                    bias_here = groups and cc > 0
                    if not (a_here or bias_here):
                        continue
                    if a_here:
                        pe.wait_ge(mats_in[cc % 2], ring_use(a_chunk, k - 1, cc) * PER_CHUNK)

                    def pair(p):
                        for half in range(2):
                            if a_here:
                                a_rows(k - 1, cc, p * 2 + (2 * PAIRS * cc + half), half, p * (2 * ROWS) + half * ROWS)
                            if bias_here:
                                bias_tile(k, p * 2 + (2 * PAIRS * (cc - 1) + half), half, groups)
                    each_pair(pe, pair, unrolled=True)
                if not groups:
                    return
                pe.wait_ge(y_ready, region_tiles(k, TILES))
                for cc in range(CHUNKS):
                    pe.wait_ge(mats_in[cc % 2], ring_use(b_chunk, k, cc) * PER_CHUNK)

                    def columns(p):
                        for half in range(2):
                            T = p * 2 + (2 * PAIRS * cc + half)
                            pe.wait_ge(main_taken, b_tile(k, T) - 1)
                            for j in range(ROWS):
                                at = p * (2 * ROWS) + (half * ROWS + j)
                                mm = pe.matmul(main[:, half, j * W:(j + 1) * W], mats[:, cc % 2, :, at],
                                               y[:, :, cc * CHUNK + at],
                                               start=True, stop=True)
                            mm.then_inc(main_ready, 1)
                    each_pair(pe, columns, unrolled=True)

            stages(pe, stage)


_INS = ["x", "L0_conv_W1", "L0_conv_b1", "L0_conv_W2", "L0_conv_b2", "L0_conv_c", "L0_conv_L_multiplier",
        "L0_conv_init_L", "L1_conv_qw1", "L1_conv_qw2", "L1_conv_kw1", "L1_conv_kw2", "L1_conv_qdd", "L1_conv_kdd",
        "L1_conv_w"]


def kernel(**inputs):
    import numpy as np
    import concourse.bacc as bacc
    from concourse.bass_utils import run_bass_kernel_spmd

    nc = bacc.Bacc("TRN2", target_bir_lowering=False, num_devices=1)
    arrays, args = {}, []
    for name in _INS:
        a = np.ascontiguousarray(inputs[name])
        if a.ndim < 2 and a.size == 1:
            a = a.reshape(1, 1)
        arrays[f"in_{name}"] = a
        args.append(nc.dram_tensor(f"in_{name}", a.shape, mybir.dt.from_np(a.dtype), kind="ExternalInput").ap())
    result = nc.dram_tensor("out_mixed", (1, H, S, S), F32, kind="ExternalOutput").ap()
    build(nc, *args, result)
    r = run_bass_kernel_spmd(nc, [arrays], core_ids=[0])
    return r.results[0]["out_mixed"]
```

```python
import concourse.bass as bass
from concourse import mybir

F32 = mybir.dt.float32
ALU = mybir.AluOpType
ACT = mybir.ActivationFunctionType

P = 128
H = 16
S = 1024
BLOCKS = P // H
W = S // BLOCKS
REGIONS = S // W
HID = 32
SLOTS = P // HID
ROWS = 8
COLS = ROWS * W
BANK = 512
CHUNK = 32
CHUNKS = W // CHUNK
RING = 4
PAIRS = CHUNK // (2 * ROWS)
TILES = W // ROWS
HALF = REGIONS // 2
SETUP_TILES = 4
TABLE = S + W - 1
DMA = 16
PER_CHUNK = BLOCKS * DMA
EPS = 1e-6


def build(nc, x, W1, b1, W2, b2, c, L_mult, init_L, qw1, qw2, kw1, kw2, qdd, kdd, w, out):
    a_mats = nc.dram_tensor("a_mats", (REGIONS, CHUNKS, H, H * CHUNK), F32, kind="Internal").ap()
    b_mats = nc.dram_tensor("b_mats", (BLOCKS, CHUNKS, H, H * CHUNK), F32, kind="Internal").ap()

    from contextlib import ExitStack
    with ExitStack() as ctx:
        def sb(name, shape):
            return ctx.enter_context(nc.sbuf_tensor(name, shape, F32))

        def sem(name):
            return ctx.enter_context(nc.semaphore(name))

        y = sb("y", [P, W, W])
        mixed = sb("mixed", [P, W, W])
        mats = sb("mats", [P, 2, P, CHUNK])
        x_last = sb("x_last", [P, CHUNK, W])
        hidden = sb("hidden", [P, RING, COLS])
        log_table = sb("log_table", [P, TABLE])
        row_scale = sb("row_scale", [P, S])
        w2_blocks = sb("w2_blocks", [P, 2, P])
        ident = sb("ident", [P, P])
        w1_col = sb("w1_col", [P, 1])
        b1_col = sb("b1_col", [P, 1])
        b2_col = sb("b2_col", [P, 2])
        relu_b1 = sb("relu_b1", [P, 1])
        zero_col = sb("zero_col", [P, 1])
        slot_col = sb("slot_col", [P, 1])
        c_col = sb("c_col", [P, 1])
        thr_col = sb("thr_col", [P, 3])

        spare = mixed[:].rearrange("p t s -> p (t s)")
        comp = {"a": spare[:, 0:2048], "b": spare[:, 2048:4096]}
        term = spare[:, 4096:6144]
        turned = {"a": spare[:, 6144:8192], "b": spare[:, 8192:10240]}
        first = {"a": spare[:, 10240:10496], "b": spare[:, 10496:10752]}
        second = {"a": spare[:, 10752:11008], "b": spare[:, 11008:11264]}
        diag = {"a": spare[:, 11264:11392], "b": spare[:, 11392:11520]}
        w_eye = spare[:, 11520:11776]

        main = ctx.enter_context(nc.psum_tensor("main", [P, 2, COLS], F32))
        bias = ctx.enter_context(nc.psum_tensor("bias", [P, 2, COLS], F32))

        weights_in = {"a": sem("weights_in_a"), "b": sem("weights_in_b")}
        consts_in = sem("consts_in")
        w2_in = sem("w2_in")
        w1_in = sem("w1_in")
        b2_in = sem("b2_in")
        zeroed = sem("zeroed")
        mats_zeroed = sem("mats_zeroed")
        indices_made = sem("indices_made")
        ident_made = sem("ident_made")
        dve_step = sem("dve_step")
        logs_wanted = sem("logs_wanted")
        logs_made = sem("logs_made")
        tables_made = sem("tables_made")
        comp_made = sem("comp_made")
        b_mats_out = sem("b_mats_out")
        a_mats_out = sem("a_mats_out")
        relu_b1_made = sem("relu_b1_made")
        const_bias_made = sem("const_bias_made")
        const_bias_read = sem("const_bias_read")

        x_in = [sem(f"x_in{i}") for i in range(CHUNKS)]
        mats_in = [sem(f"mats_in{i}") for i in range(2)]
        nd_ready = sem("nd_ready")
        nd_dve_ready = sem("nd_dve_ready")
        hidden_ready = sem("hidden_ready")
        hidden_used = sem("hidden_used")
        y_ready = sem("y_ready")
        main_ready = sem("main_ready")
        main_taken = sem("main_taken")
        out_done = sem("out_done")

        def region_tiles(k, T):
            return k * TILES + T

        def hidden_index(k, T, g, groups):
            if groups == 1:
                return k * TILES + T
            return (k - HALF) * (2 * TILES) + (HALF * TILES + g) + T * 2

        def hidden_slot(p, half, g, groups):
            return p * 2 + half if groups == 1 else 2 * half + g

        def nd_by_dve(T_half, g, groups):
            return groups == 2 and T_half == 1 and g == 1

        def nd_index(k, pair_of_tiles, T_half, g, groups):
            if groups == 1:
                return k * TILES + pair_of_tiles * 2 + T_half
            if nd_by_dve(T_half, g, groups):
                return (k - HALF) * (TILES // 2) + pair_of_tiles
            return (k - HALF) * (3 * TILES // 2) + pair_of_tiles * 3 + (HALF * TILES + 2 * T_half + g)

        def make_nd(eng, dst, t0, g):
            logs = log_table[:, bass.ds(t0 - SLOTS * W * g, ROWS)]
            scales = row_scale[:, bass.ds(t0, ROWS)]
            return eng.tensor_tensor(dst.rearrange("p (j s) -> p j s", j=ROWS),
                                     bass.AP(logs.tensor, logs.offset, [list(logs.ap[0]), [1, ROWS], [1, W]]),
                                     bass.AP(scales.tensor, scales.offset, [list(scales.ap[0]), [1, ROWS], [0, W]]),
                                     ALU.mult)

        def b_tile(k, T):
            return k * (2 * TILES) + (SETUP_TILES + T)

        def a_tile(k, T):
            return k * (2 * TILES) + (SETUP_TILES + TILES + T)

        def b_chunk(k, cc):
            return k * (2 * CHUNKS) + cc

        def a_chunk(k, cc):
            return k * (2 * CHUNKS) + (CHUNKS + cc)

        def tiles_before(chunk):
            return chunk * (2 * PAIRS) + SETUP_TILES

        def ring_use(chunk_of, k, cc):
            return k * CHUNKS + (chunk_of(0, cc) // 2 + 1)

        def wait(eng, semaphore, count):
            if not (isinstance(count, int) and count <= 0):
                eng.wait_ge(semaphore, count)

        def each_pair(eng, body, unrolled=False):
            if unrolled:
                for p in range(PAIRS):
                    body(p)
            else:
                with eng.Fori(0, PAIRS) as p:
                    body(p)

        def stages(eng, stage):
            stage(0, mix_a=False, groups=1)
            with eng.Fori(1, HALF) as k:
                stage(k, mix_a=True, groups=1)
            with eng.Fori(HALF, REGIONS) as k:
                stage(k, mix_a=True, groups=2)
            stage(REGIONS, mix_a=True, groups=0)

        def rows(tile, first_row, n):
            return tile[:, bass.ds(first_row, n), :].rearrange("p t s -> p (t s)")

        def slot_of(ring, slot):
            return ring[:, bass.ds(slot, 1), :].rearrange("p o c -> p (o c)")

        block = ctx.enter_context(nc.Block())

        @block.sync
        def _(sp):
            def load_compact(part, v1, v2, vd):
                for dst, src in ((first[part], v1), (second[part], v2)):
                    sp.dma_start(dst.rearrange("p (b i) -> p b i", b=BLOCKS),
                                 src.rearrange("o (b p) g i m -> p (o b) (g i m)", p=P)).then_inc(weights_in[part], DMA)
                sp.dma_start(diag[part].rearrange("p (b m) -> p b m", b=BLOCKS),
                             vd.rearrange("o (b p) g m -> p (o b) (g m)", p=P)).then_inc(weights_in[part], DMA)

            def load_biases():
                for q in range(SLOTS):
                    part = slice(HID * q, HID * (q + 1))
                    sp.dma_start(w1_col[part, :], W1.rearrange("o m -> m o")).then_inc(w1_in, DMA)
                    sp.dma_start(b1_col[part, :], b1.rearrange("(m o) -> m o", o=1)).then_inc(w1_in, DMA)

            sp.dma_start(c_col[:], c.partition_broadcast(P)).then_inc(consts_in, DMA)
            sp.dma_start(thr_col[:, 0:1], L_mult.partition_broadcast(P)).then_inc(consts_in, DMA)
            sp.dma_start(thr_col[:, 1:2], init_L.partition_broadcast(P)).then_inc(consts_in, DMA)
            load_compact("b", kw1, kw2, kdd)
            load_biases()

            def load_x(k, cc):
                into = x_last[:] if cc == CHUNKS - 1 else y[:, cc * CHUNK:(cc + 1) * CHUNK, :]
                for b in range(BLOCKS):
                    sp.dma_start(into[H * b:H * (b + 1)],
                                 x[0, :, bass.ds(k * W + cc * CHUNK, CHUNK), b * W:(b + 1) * W]).then_inc(x_in[cc], DMA)

            def store(k, cc):
                sp.wait_ge(main_taken, tiles_before(a_chunk(k, cc) + 1))
                for b in range(BLOCKS):
                    sp.dma_start(out[0, :, bass.ds(k * W + cc * CHUNK, CHUNK), b * W:(b + 1) * W],
                                 mixed[H * b:H * (b + 1), cc * CHUNK:(cc + 1) * CHUNK, :]).then_inc(out_done, DMA)

            def load_mats(chunk_of, k, cc):
                sp.wait_ge(main_ready, tiles_before(chunk_of(k, cc) - 1))
                slot = cc % 2
                for b in range(BLOCKS):
                    dst = mats[H * b:H * (b + 1), slot, H * b:H * (b + 1), :].rearrange("p n e -> p (n e)")
                    if chunk_of is b_chunk:
                        src = b_mats[b, cc]
                    else:
                        src = a_mats[bass.ds(k, 1), cc].rearrange("o m f -> (o m) f")
                    sp.dma_start(dst, src).then_inc(mats_in[slot], DMA)

            def stage(k, mix_a, groups):
                if mix_a:
                    if groups:
                        sp.wait_ge(y_ready, region_tiles(k, 0))
                        load_x(k, CHUNKS - 1)
                    load_mats(a_chunk, k - 1, 0)
                    load_mats(a_chunk, k - 1, 1)
                else:
                    load_x(k, 0)
                    sp.wait_ge(zeroed, 2)
                    for q in range(SLOTS):
                        sp.dma_start(bass.AP(w2_blocks, HID * q * 2 * P + H * q, [[2 * P, HID], [P + P // 2, 2], [1, H]]),
                                     bass.AP(W2.tensor, W2.offset, [[H, HID], [0, 2], [1, H]])).then_inc(w2_in, DMA)
                    load_compact("a", qw1, qw2, qdd)
                    sp.dma_start(w_eye, w.rearrange("g m n -> g (m n)").partition_broadcast(P))\
                        .then_inc(weights_in["a"], DMA)
                    for b in range(BLOCKS):
                        sp.dma_start(b2_col[H * b:H * (b + 1), 0:1], b2.rearrange("(h o) -> h o", o=1)).then_inc(b2_in, DMA)
                    for cc in range(1, CHUNKS):
                        load_x(k, cc)
                    for part, mat, done in (("b", b_mats, b_mats_out), ("a", a_mats, a_mats_out)):
                        for half in range(2):
                            sp.wait_ge(main_taken, 2 * (part == "a") + half + 1)
                            src = turned[part][:, half * COLS:(half + 1) * COLS].rearrange("p (j e) -> p j e", e=CHUNK)
                            dst = mat[:, :, half * (H // 2):(half + 1) * (H // 2), :].rearrange(
                                "b j m (n e) -> (m n) (b j) e", e=CHUNK)
                            sp.dma_start(dst, src).then_inc(done, DMA)
                    sp.wait_ge(b_mats_out, 2 * DMA)
                    sp.wait_ge(mats_zeroed, 2)
                for cc in range(CHUNKS):
                    if mix_a:
                        if groups and cc < CHUNKS - 1:
                            sp.wait_ge(main_ready, tiles_before(a_chunk(k - 1, cc) + 1))
                            load_x(k, cc)
                        if cc + 2 < CHUNKS:
                            load_mats(a_chunk, k - 1, cc + 2)
                        elif groups:
                            load_mats(b_chunk, k, cc + 2 - CHUNKS)
                        store(k - 1, cc)
                    elif cc < 2:
                        load_mats(b_chunk, k, cc)
                if groups:
                    load_mats(b_chunk, k, 2)
                    load_mats(b_chunk, k, 3)
                if not mix_a:
                    sp.wait_ge(a_mats_out, 2 * DMA)

            stages(sp, stage)
            sp.wait_ge(out_done, REGIONS * CHUNKS * PER_CHUNK)

        @block.gpsimd
        def _(pool):
            nc.gpsimd.iota(log_table[:], pattern=[[1, TABLE]], base=-(W - 1), channel_multiplier=0,
                           allow_small_or_imprecise_dtypes=True).then_inc(indices_made, 1)
            pool.wait_ge(indices_made, 1)
            for q in range(SLOTS):
                nc.gpsimd.iota(slot_col[HID * q:HID * (q + 1), :], pattern=[[1, 1]], base=W * q,
                               channel_multiplier=0, allow_small_or_imprecise_dtypes=True).then_inc(indices_made, 1)
            pool.wait_ge(indices_made, SLOTS + 1)
            nc.gpsimd.memset(ident[:], 0.0).then_inc(ident_made, 1)
            pool.wait_ge(ident_made, 1)
            nc.gpsimd.affine_select(out=ident[:], in_=ident[:], compare_op=ALU.not_equal, fill=1.0, base=0,
                                    pattern=[[-1, P]], channel_multiplier=1).then_inc(ident_made, 1)
            pool.wait_ge(ident_made, 2)
            pool.wait_ge(tables_made, 1)
            pool.wait_ge(logs_made, 2)

            def stage(k, mix_a, groups):
                if not groups:
                    return
                for cc in range(CHUNKS):
                    def pair(p):
                        for half in range(2):
                            T = p * 2 + (2 * PAIRS * cc + half)
                            for g in range(groups):
                                if nd_by_dve(half, g, groups):
                                    continue
                                wait(pool, hidden_used, hidden_index(k, T, g, groups) - (RING - 1))
                                make_nd(pool, slot_of(hidden, hidden_slot(p, half, g, groups)), k * W + T * ROWS, g)\
                                    .then_inc(nd_ready, 1)
                    each_pair(pool, pair, unrolled=(not mix_a and cc == 0))

            stages(pool, stage)

        @block.scalar
        def _(act):
            def zero_mats(slot):
                part = mats[:, slot].rearrange("p n e -> p (n e)")
                nc.scalar.activation(part, zero_col[:].to_broadcast([P, P * CHUNK]), ACT.Copy).then_inc(mats_zeroed, 1)

            act.wait_ge(zeroed, 1)
            zero_mats(0)
            act.wait_ge(logs_wanted, 1)
            nc.scalar.activation(row_scale[:], row_scale[:], ACT.Ln, bias=1.0, scale=c_col[:, 0:1]).then_inc(logs_made, 1)
            act.wait_ge(logs_wanted, 2)
            nc.scalar.activation(log_table[:], log_table[:], ACT.Ln, bias=1.0, scale=c_col[:, 0:1]).then_inc(logs_made, 1)
            act.wait_ge(w1_in, 2 * SLOTS * DMA)
            nc.scalar.activation(relu_b1[:], b1_col[:], ACT.Relu).then_inc(relu_b1_made, 1)
            zero_mats(1)

            def turn_out(part, half):
                act.wait_ge(main_ready, 2 * (part == "a") + half + 1)
                nc.scalar.activation(turned[part][:, half * COLS:(half + 1) * COLS], slot_of(main, half), ACT.Copy)\
                    .then_inc(main_taken, 1)

            def stage(k, mix_a, groups):
                if not groups:
                    return
                for cc in range(CHUNKS):
                    def pair(p):
                        for half in range(2):
                            T = p * 2 + (2 * PAIRS * cc + half)
                            for g in range(groups):
                                made = nd_index(k, p + PAIRS * cc, half, g, groups)
                                act.wait_ge(nd_dve_ready if nd_by_dve(half, g, groups) else nd_ready, made + 1)
                                tile = slot_of(hidden, hidden_slot(p, half, g, groups))
                                nc.scalar.activation(tile, tile, ACT.Relu, bias=b1_col[:, 0:1],
                                                     scale=w1_col[:, 0:1]).then_inc(hidden_ready, 1)
                    each_pair(act, pair, unrolled=(not mix_a and cc == 0))
                    if not mix_a and cc in (0, CHUNKS - 1):
                        part = "b" if cc == 0 else "a"
                        turn_out(part, 0)
                        turn_out(part, 1)
                if mix_a:
                    act.wait_ge(out_done, k * (CHUNKS * PER_CHUNK))
                else:
                    act.wait_ge(b_mats_out, 2 * DMA)
                    act.wait_ge(a_mats_out, 2 * DMA)
                with act.Fori(0, TILES // 2) as p:
                    for half in range(2):
                        T = p * 2 + half
                        act.wait_ge(main_ready, b_tile(k, T) + 1)
                        nc.scalar.activation(mixed[:, :, bass.ds(T * ROWS, ROWS)],
                                             slot_of(main, half).rearrange("p (s t) -> p t s", s=ROWS),
                                             ACT.Copy).then_inc(main_taken, 1)

            stages(act, stage)

        @block.vector
        def _(dve):
            steps = [0]

            def step(instruction):
                steps[0] += 1
                instruction.then_inc(dve_step, 1)
                dve.wait_ge(dve_step, steps[0])

            def absolute(ap):
                return dve.scalar_tensor_tensor(out=ap, in0=ap, scalar=-1.0, in1=ap, op0=ALU.mult, op1=ALU.max)

            dve.memset(zero_col[:], 0.0).then_inc(zeroed, 1)
            dve.memset(w2_blocks[:], 0.0).then_inc(zeroed, 1)
            dve.wait_ge(consts_in, 3 * DMA)
            step(absolute(c_col[:]))
            step(dve.tensor_tensor(thr_col[:, 2:3], thr_col[:, 0:1], thr_col[:, 1:2], ALU.mult))
            step(absolute(thr_col[:, 2:3]))
            dve.wait_ge(indices_made, SLOTS + 1)
            step(dve.tensor_scalar(row_scale[:], log_table[:, W - 1:], thr_col[:, 2:3], None, ALU.max))
            dve.sem_inc(logs_wanted, 1)
            dve.tensor_scalar(log_table[:], log_table[:], slot_col[:, 0:1], 0.0, ALU.subtract, ALU.max)\
               .then_inc(logs_wanted, 1)

            def square(ap):
                return ap.rearrange("p (b m n) -> p b m n", b=BLOCKS, m=H)

            def rank_one(part, i, dst):
                shape = [P, BLOCKS, H, H]
                u = first[part].rearrange("p (b i m) -> p b i m", b=BLOCKS, i=2)[:, :, i, :]
                v = second[part].rearrange("p (b i m) -> p b i m", b=BLOCKS, i=2)[:, :, i, :]
                return dve.tensor_tensor(square(dst), u.unsqueeze(3).to_broadcast(shape),
                                         v.unsqueeze(2).to_broadcast(shape), ALU.mult)

            def diagonal(ap, blocks):
                return bass.AP(ap.tensor, ap.offset, [list(ap.ap[0]), [H * H, blocks], [H + 1, H]])

            def compact(part):
                dve.wait_ge(weights_in[part], DMA * (3 + (part == "a")))
                if part == "a":
                    eye = diagonal(w_eye, 1)
                    step(dve.tensor_scalar(eye, eye, 1.0, None, ALU.add))
                rank_one(part, 0, comp[part])
                step(rank_one(part, 1, term))
                step(dve.tensor_tensor(comp[part], comp[part], term, ALU.add))
                if part == "a":
                    whole = comp[part].rearrange("p (b f) -> p b f", b=BLOCKS)
                    step(dve.tensor_tensor(whole, whole, w_eye.unsqueeze(1).to_broadcast([P, BLOCKS, H * H]), ALU.add))
                on = diagonal(comp[part], BLOCKS)
                dve.tensor_tensor(on, on, diag[part].rearrange("p (b m) -> p b m", b=BLOCKS), ALU.add)\
                   .then_inc(comp_made, 1)

            dve.wait_ge(logs_made, 1)
            step(dve.tensor_scalar(row_scale[:], row_scale[:], EPS, None, ALU.add))
            dve.reciprocal(row_scale[:], row_scale[:]).then_inc(tables_made, 1)
            compact("b")
            compact("a")
            dve.wait_ge(b2_in, BLOCKS * DMA)
            step(dve.tensor_copy(b2_col[:, 1:2], b2_col[:, 0:1]))
            dve.wait_ge(const_bias_made, 1)
            dve.tensor_tensor(b2_col[P // 2:, 1:2], b2_col[P // 2:, 0:1], bias[P // 2:, 1, 0:1], ALU.add)\
               .then_inc(const_bias_read, 1)
            dve.wait_ge(const_bias_read, 1)

            def finish_tile(k, T, half):
                dve.wait_ge(main_taken, b_tile(k, TILES - 1) + 1)
                dve.wait_ge(main_ready, a_tile(k, T) + 1)
                dve.tensor_tensor(rows(mixed, T * ROWS, ROWS), slot_of(main, half), rows(mixed, T * ROWS, ROWS),
                                  ALU.add).then_inc(main_taken, 1)

            def add_bias(k, cc, T, half, groups):
                dve.wait_ge(x_in[cc], k * PER_CHUNK + PER_CHUNK)
                dve.wait_ge(hidden_used, hidden_index(k, T, groups - 1, groups) + 1)
                falling = bass.AP(bias, half * COLS + W - 1, [[2 * COLS, P], [W, ROWS], [-1, W]])
                y_rows = y[:, bass.ds(T * ROWS, ROWS), :]
                x_rows = x_last[:, bass.ds(T * ROWS - cc * CHUNK, ROWS), :] if cc == CHUNKS - 1 else y_rows
                dve.scalar_tensor_tensor(out=y_rows, in0=falling, scalar=b2_col[:, 2 - groups:3 - groups], in1=x_rows,
                                         op0=ALU.add, op1=ALU.add).then_inc(y_ready, 1)

            def stage(k, mix_a, groups):
                for cc in range(CHUNKS + 1):
                    a_here = mix_a and cc < CHUNKS
                    bias_here = groups and cc > 0
                    if not (a_here or bias_here):
                        continue

                    def pair(p):
                        if bias_here and groups == 2:
                            T = p * 2 + (2 * PAIRS * (cc - 1) + 1)
                            dve.wait_ge(hidden_used, hidden_index(k, T, 1, groups) - (RING - 1))
                            make_nd(dve, slot_of(hidden, hidden_slot(p, 1, 1, groups)), k * W + T * ROWS, 1)\
                                .then_inc(nd_dve_ready, 1)
                        for half in range(2):
                            if a_here:
                                finish_tile(k - 1, p * 2 + (2 * PAIRS * cc + half), half)
                            if bias_here:
                                add_bias(k, cc - 1, p * 2 + (2 * PAIRS * (cc - 1) + half), half, groups)
                    each_pair(dve, pair)

            stages(dve, stage)

        @block.tensor
        def _(pe):
            def transposes(part):
                pe.wait_ge(comp_made, 1 + (part == "a"))
                for half in range(2):
                    wait(pe, main_taken, 2 * (part == "a") + half - 1)
                    for b in range(BLOCKS):
                        at = (2 * b + half) * P
                        mm = pe.transpose(main[:, half, b * P:(b + 1) * P], comp[part][:, at:at + P], ident[:])
                    mm.then_inc(main_ready, 1)

            pe.wait_ge(ident_made, 2)
            transposes("b")
            pe.wait_ge(w2_in, SLOTS * DMA)
            pe.wait_ge(relu_b1_made, 1)
            for g in range(2):
                mm = pe.matmul(bias[:, 1, 0:1], w2_blocks[:, g, :], relu_b1[:, 0:1], start=(g == 0), stop=(g == 1))
            mm.then_inc(const_bias_made, 1)
            pe.wait_ge(const_bias_read, 1)

            def a_rows(k, cc, T, half, first_row):
                pe.wait_ge(main_taken, a_tile(k, T) - 1)
                for j in range(ROWS):
                    mm = pe.matmul(main[:, half, j * W:(j + 1) * W],
                                   mats[:, cc % 2, :, first_row + j], y[:, T * ROWS + j, :], start=True, stop=True)
                mm.then_inc(main_ready, 1)

            def bias_tile(k, p, T, half, groups):
                wait(pe, y_ready, region_tiles(k, T) - 1)
                pe.wait_ge(hidden_ready, hidden_index(k, T, groups - 1, groups) + 1)
                for at in range(0, COLS, BANK):
                    for g in range(groups):
                        part = slice(0, P) if groups == 1 else slice(P // 2 * g, P // 2 * (g + 1))
                        mm = pe.matmul(bias[part, half, at:at + BANK], w2_blocks[:, g, part],
                                       hidden[:, hidden_slot(p, half, g, groups), at:at + BANK],
                                       start=True, stop=True)
                        if at == COLS - BANK:
                            mm.then_inc(hidden_used, 1)

            def stage(k, mix_a, groups):
                for cc in range(CHUNKS + 1):
                    a_here = mix_a and cc < CHUNKS
                    bias_here = groups and cc > 0
                    if not (a_here or bias_here):
                        continue
                    if a_here:
                        pe.wait_ge(mats_in[cc % 2], ring_use(a_chunk, k - 1, cc) * PER_CHUNK)

                    def pair(p):
                        for half in range(2):
                            if a_here:
                                a_rows(k - 1, cc, p * 2 + (2 * PAIRS * cc + half), half, p * (2 * ROWS) + half * ROWS)
                            if bias_here:
                                bias_tile(k, p, p * 2 + (2 * PAIRS * (cc - 1) + half), half, groups)
                    each_pair(pe, pair, unrolled=True)
                if not groups:
                    return
                if not mix_a:
                    transposes("a")
                pe.wait_ge(y_ready, region_tiles(k, TILES))
                for cc in range(CHUNKS):
                    pe.wait_ge(mats_in[cc % 2], ring_use(b_chunk, k, cc) * PER_CHUNK)

                    def columns(p):
                        for half in range(2):
                            T = p * 2 + (2 * PAIRS * cc + half)
                            pe.wait_ge(main_taken, b_tile(k, T) - 1)
                            for j in range(ROWS):
                                at = p * (2 * ROWS) + (half * ROWS + j)
                                mm = pe.matmul(main[:, half, j * W:(j + 1) * W], mats[:, cc % 2, :, at],
                                               y[:, :, cc * CHUNK + at],
                                               start=True, stop=True)
                            mm.then_inc(main_ready, 1)
                    each_pair(pe, columns, unrolled=True)

            stages(pe, stage)


_INS = ["x", "L0_conv_W1", "L0_conv_b1", "L0_conv_W2", "L0_conv_b2", "L0_conv_c", "L0_conv_L_multiplier",
        "L0_conv_init_L", "L1_conv_qw1", "L1_conv_qw2", "L1_conv_kw1", "L1_conv_kw2", "L1_conv_qdd", "L1_conv_kdd",
        "L1_conv_w"]


def kernel(**inputs):
    import numpy as np
    import concourse.bacc as bacc
    from concourse.bass_utils import run_bass_kernel_spmd

    nc = bacc.Bacc("TRN2", target_bir_lowering=False, num_devices=1)
    arrays, args = {}, []
    for name in _INS:
        a = np.ascontiguousarray(inputs[name])
        if a.ndim < 2 and a.size == 1:
            a = a.reshape(1, 1)
        arrays[f"in_{name}"] = a
        args.append(nc.dram_tensor(f"in_{name}", a.shape, mybir.dt.from_np(a.dtype), kind="ExternalInput").ap())
    result = nc.dram_tensor("out_mixed", (1, H, S, S), F32, kind="ExternalOutput").ap()
    build(nc, *args, result)
    r = run_bass_kernel_spmd(nc, [arrays], core_ids=[0])
    return r.results[0]["out_mixed"]
```

```python
import concourse.bass as bass
from concourse import mybir

F32 = mybir.dt.float32
ALU = mybir.AluOpType
ACT = mybir.ActivationFunctionType

P = 128
H = 16
S = 1024
BLOCKS = P // H
W = S // BLOCKS
REGIONS = S // W
HID = 32
SLOTS = P // HID
ROWS = 8
COLS = ROWS * W
BANK = 512
CHUNK = 32
CHUNKS = W // CHUNK
BIAS_LAG = 5
RING = 4
PAIRS = CHUNK // (2 * ROWS)
EARLY = 2
TILES = W // ROWS
HALF = REGIONS // 2
SETUP_TILES = 2
TABLE = S + W - 1
DMA = 16
PER_CHUNK = BLOCKS * DMA
EPS = 1e-6


def build(nc, x, W1, b1, W2, b2, c, L_mult, init_L, qw1, qw2, kw1, kw2, qdd, kdd, w, out):
    a_mats = nc.dram_tensor("a_mats", (REGIONS, CHUNKS, H, H * CHUNK), F32, kind="Internal").ap()
    b_mats = nc.dram_tensor("b_mats", (BLOCKS, CHUNKS, H, H * CHUNK), F32, kind="Internal").ap()

    from contextlib import ExitStack
    with ExitStack() as ctx:
        def sb(name, shape):
            return ctx.enter_context(nc.sbuf_tensor(name, shape, F32))

        def sem(name):
            return ctx.enter_context(nc.semaphore(name))

        y = sb("y", [P, W, W])
        mixed = sb("mixed", [P, W, W])
        mats = sb("mats", [P, 2, P, CHUNK])
        x_last = sb("x_last", [P, CHUNK, W])
        hidden = sb("hidden", [P, RING, COLS])
        log_table = sb("log_table", [P, TABLE])
        row_scale = sb("row_scale", [P, S])
        w2_blocks = sb("w2_blocks", [P, 2, P])
        ident = sb("ident", [P, P])
        w1_col = sb("w1_col", [P, 1])
        b1_col = sb("b1_col", [P, 1])
        b2_col = sb("b2_col", [P, 2])
        relu_b1 = sb("relu_b1", [P, 1])
        zero_col = sb("zero_col", [P, 1])
        slot_col = sb("slot_col", [P, 1])
        c_col = sb("c_col", [P, 1])
        thr_col = sb("thr_col", [P, 3])

        a_inputs = sb("a_inputs", [P, 896])
        spare_b = mixed[:].rearrange("p t s -> p (t s)")
        spare_a = x_last[:].rearrange("p t s -> p (t s)")
        comp = {"a": spare_a[:, 0:2048], "b": spare_b[:, 0:2048]}
        term = {"a": spare_a[:, 2048:4096], "b": spare_b[:, 2048:4096]}
        turned = {"a": term["a"], "b": spare_b[:, 8192:10240]}
        first = {"a": a_inputs[:, 0:256], "b": spare_b[:, 10240:10496]}
        second = {"a": a_inputs[:, 256:512], "b": spare_b[:, 10496:10752]}
        diag = {"a": a_inputs[:, 512:640], "b": spare_b[:, 10752:10880]}
        w_eye = a_inputs[:, 640:896]

        main = ctx.enter_context(nc.psum_tensor("main", [P, 2, COLS], F32))
        bias = ctx.enter_context(nc.psum_tensor("bias", [P, 2, COLS], F32))

        weights_in = {"a": sem("weights_in_a"), "b": sem("weights_in_b")}
        consts_in = sem("consts_in")
        w2_in = sem("w2_in")
        w1_in = sem("w1_in")
        b2_in = sem("b2_in")
        zeroed = sem("zeroed")
        mats_zeroed = sem("mats_zeroed")
        indices_made = sem("indices_made")
        ident_made = sem("ident_made")
        dve_step = sem("dve_step")
        logs_wanted = sem("logs_wanted")
        logs_made = sem("logs_made")
        tables_made = sem("tables_made")
        comp_made = sem("comp_made")
        a_transposed = sem("a_transposed")
        a_turned = sem("a_turned")
        b_mats_out = sem("b_mats_out")
        a_mats_out = sem("a_mats_out")
        relu_b1_made = sem("relu_b1_made")
        table_loaded = sem("table_loaded")
        const_bias_made = sem("const_bias_made")
        const_bias_read = sem("const_bias_read")

        x_in = [sem(f"x_in{i}") for i in range(CHUNKS)]
        mats_in = [sem(f"mats_in{i}") for i in range(2)]
        nd_ready = sem("nd_ready")
        nd_dve_ready = sem("nd_dve_ready")
        hidden_ready = sem("hidden_ready")
        hidden_used = sem("hidden_used")
        first_bank_ready = sem("first_bank_ready")
        y_ready = sem("y_ready")
        y_const_ready = sem("y_const_ready")
        main_ready = sem("main_ready")
        main_taken = sem("main_taken")
        early_out = sem("early_out")
        late_out = sem("late_out")

        def region_tiles(k, T):
            return k * TILES + T

        def hidden_index(k, T, g, groups):
            if groups == 1:
                return k * TILES + T
            return (k - HALF) * (2 * TILES) + (HALF * TILES + g) + T * 2

        def in_ring(cc):
            return cc < CHUNKS - 1

        def hidden_tile(cc, p, half, g, groups):
            if in_ring(cc):
                return slot_of(hidden, p * 2 + half if groups == 1 else 2 * half + g)
            return rows(mixed, p * (2 * groups * ROWS) + (half * groups + g) * ROWS, ROWS)

        def wait_hidden_free(eng, k, cc, T, g, groups):
            if in_ring(cc):
                wait(eng, hidden_used, hidden_index(k, T, g, groups) - (RING - 1))
            elif isinstance(k, int):
                eng.wait_ge(main_ready, SETUP_TILES)
            else:
                eng.wait_ge(early_out, k * (EARLY * PER_CHUNK))

        def nd_by_dve(cc, T_half, g, groups):
            return groups == 2 and g == 1 and (T_half == 1 or cc == CHUNKS - 1)

        def nd_index(k, cc, p, T_half, g, groups):
            if groups == 1:
                return k * TILES + p * 2 + (cc * 2 * PAIRS + T_half)
            last = cc == CHUNKS - 1
            per_region = TILES // 2 + PAIRS
            if nd_by_dve(cc, T_half, g, groups):
                return (k - HALF) * per_region + p * (1 + last) + (cc * PAIRS + (T_half if last else 0))
            return ((k - HALF) * (2 * TILES - per_region) + p * (3 - last)
                    + (HALF * TILES + cc * PAIRS * 3 + (2 - last) * T_half + g))

        def make_nd(eng, dst, t0, g):
            logs = log_table[:, bass.ds(t0 - SLOTS * W * g, ROWS)]
            scales = row_scale[:, bass.ds(t0, ROWS)]
            return eng.tensor_tensor(dst.rearrange("p (j s) -> p j s", j=ROWS),
                                     bass.AP(logs.tensor, logs.offset, [list(logs.ap[0]), [1, ROWS], [1, W]]),
                                     bass.AP(scales.tensor, scales.offset, [list(scales.ap[0]), [1, ROWS], [0, W]]),
                                     ALU.mult)

        def b_tile(k, T):
            return k * (2 * TILES) + (SETUP_TILES + T)

        def a_tile(k, T):
            return k * (2 * TILES) + (SETUP_TILES + TILES + T)

        def b_chunk(k, cc):
            return k * (2 * CHUNKS) + cc

        def a_chunk(k, cc):
            return k * (2 * CHUNKS) + (CHUNKS + cc)

        def tiles_before(chunk):
            return chunk * (2 * PAIRS) + SETUP_TILES

        def ring_use(chunk_of, k, cc):
            return k * CHUNKS + (chunk_of(0, cc) // 2 + 1)

        def wait(eng, semaphore, count):
            if not (isinstance(count, int) and count <= 0):
                eng.wait_ge(semaphore, count)

        def each_pair(eng, body, unrolled=False):
            if unrolled:
                for p in range(PAIRS):
                    body(p)
            else:
                with eng.Fori(0, PAIRS) as p:
                    body(p)

        def stages(eng, stage):
            stage(0, mix_a=False, groups=1)
            with eng.Fori(1, HALF) as k:
                stage(k, mix_a=True, groups=1)
            with eng.Fori(HALF, REGIONS) as k:
                stage(k, mix_a=True, groups=2)
            stage(REGIONS, mix_a=True, groups=0)

        def stage_steps(mix_a, groups):
            if not mix_a:
                return [(None, [T]) for T in range(TILES)]
            if not groups:
                return [(T, []) for T in range(TILES)]
            return ([(T, [T - BIAS_LAG] if T >= BIAS_LAG else []) for T in range(TILES)]
                    + [(None, [T]) for T in range(TILES - BIAS_LAG, TILES)])

        low_half, high_half = slice(0, P // 2), slice(P // 2, P)

        def rows(tile, first_row, n):
            return tile[:, bass.ds(first_row, n), :].rearrange("p t s -> p (t s)")

        def slot_of(ring, slot):
            return ring[:, bass.ds(slot, 1), :].rearrange("p o c -> p (o c)")

        block = ctx.enter_context(nc.Block())

        @block.sync
        def _(sp):
            def load_compact(part, v1, v2, vd):
                for dst, src in ((first[part], v1), (second[part], v2)):
                    sp.dma_start(dst.rearrange("p (b i) -> p b i", b=BLOCKS),
                                 src.rearrange("o (b p) g i m -> p (o b) (g i m)", p=P)).then_inc(weights_in[part], DMA)
                sp.dma_start(diag[part].rearrange("p (b m) -> p b m", b=BLOCKS),
                             vd.rearrange("o (b p) g m -> p (o b) (g m)", p=P)).then_inc(weights_in[part], DMA)

            def load_biases():
                for col, vector, n, done in ((w1_col, W1, HID, w1_in), (b1_col, b1, HID, w1_in), (b2_col, b2, H, b2_in)):
                    sp.dma_start(col[:, 0:1], bass.AP(vector.tensor, vector.offset, [[0, P // n], [1, n], [1, 1]]))\
                        .then_inc(done, DMA)

            sp.dma_start(c_col[:], c.partition_broadcast(P)).then_inc(consts_in, DMA)
            sp.dma_start(thr_col[:, 0:1], L_mult.partition_broadcast(P)).then_inc(consts_in, DMA)
            sp.dma_start(thr_col[:, 1:2], init_L.partition_broadcast(P)).then_inc(consts_in, DMA)
            load_compact("b", kw1, kw2, kdd)
            load_biases()

            def load_x(k, cc):
                into = x_last[:] if cc == CHUNKS - 1 else y[:, cc * CHUNK:(cc + 1) * CHUNK, :]
                for b in range(BLOCKS):
                    sp.dma_start(into[H * b:H * (b + 1)],
                                 x[0, :, bass.ds(k * W + cc * CHUNK, CHUNK), b * W:(b + 1) * W]).then_inc(x_in[cc], DMA)

            def store(k, cc):
                sp.wait_ge(main_taken, tiles_before(a_chunk(k, cc) + 1))
                for b in range(BLOCKS):
                    sp.dma_start(out[0, :, bass.ds(k * W + cc * CHUNK, CHUNK), b * W:(b + 1) * W],
                                 mixed[H * b:H * (b + 1), cc * CHUNK:(cc + 1) * CHUNK, :])\
                        .then_inc(early_out if cc < EARLY else late_out, DMA)

            def load_mats(chunk_of, k, cc):
                wait(sp, main_ready, tiles_before(chunk_of(k, cc) - 1))
                slot = cc % 2
                for b in range(BLOCKS):
                    dst = mats[H * b:H * (b + 1), slot, H * b:H * (b + 1), :].rearrange("p n e -> p (n e)")
                    if chunk_of is b_chunk:
                        src = b_mats[b, cc]
                    else:
                        src = a_mats[bass.ds(k, 1), cc].rearrange("o m f -> (o m) f")
                    sp.dma_start(dst, src).then_inc(mats_in[slot], DMA)

            def save_mats(part, mat, taken, done):
                for half in range(2):
                    sp.wait_ge(taken, half + 1)
                    src = turned[part][:, half * COLS:(half + 1) * COLS].rearrange("p (j e) -> p j e", e=CHUNK)
                    dst = mat[:, :, half * (H // 2):(half + 1) * (H // 2), :].rearrange(
                        "b j m (n e) -> (m n) (b j) e", e=CHUNK)
                    sp.dma_start(dst, src).then_inc(done, DMA)

            def stage(k, mix_a, groups):
                if mix_a:
                    if groups:
                        sp.wait_ge(main_ready, b_tile(k - 1, 0) + 1)
                        load_x(k, CHUNKS - 1)
                    load_mats(a_chunk, k - 1, 0)
                    load_mats(a_chunk, k - 1, 1)
                else:
                    sp.wait_ge(zeroed, 2)
                    for q in range(SLOTS):
                        sp.dma_start(bass.AP(w2_blocks, HID * q * 2 * P + H * q, [[2 * P, HID], [P + P // 2, 2], [1, H]]),
                                     bass.AP(W2.tensor, W2.offset, [[H, HID], [0, 2], [1, H]])).then_inc(w2_in, DMA)
                    for cc in range(2):
                        load_x(k, cc)
                    load_compact("a", qw1, qw2, qdd)
                    sp.dma_start(w_eye, w.rearrange("g m n -> g (m n)").partition_broadcast(P))\
                        .then_inc(weights_in["a"], DMA)
                    for cc in range(2, CHUNKS):
                        load_x(k, cc)
                    save_mats("b", b_mats, main_taken, b_mats_out)
                    sp.wait_ge(b_mats_out, 2 * DMA)
                    sp.wait_ge(mats_zeroed, 2)
                for cc in range(CHUNKS):
                    if mix_a:
                        if groups and cc < CHUNKS - 1:
                            sp.wait_ge(main_ready, tiles_before(a_chunk(k - 1, cc) + 1))
                            load_x(k, cc)
                        if cc + 2 < CHUNKS:
                            load_mats(a_chunk, k - 1, cc + 2)
                        elif groups:
                            load_mats(b_chunk, k, cc + 2 - CHUNKS)
                        store(k - 1, cc)
                    elif cc < 2:
                        load_mats(b_chunk, k, cc)
                if groups:
                    load_mats(b_chunk, k, 2)
                    if not mix_a:
                        save_mats("a", a_mats, a_turned, a_mats_out)
                    load_mats(b_chunk, k, 3)
                if not mix_a:
                    sp.wait_ge(a_mats_out, 2 * DMA)

            stages(sp, stage)
            sp.wait_ge(early_out, REGIONS * EARLY * PER_CHUNK)
            sp.wait_ge(late_out, REGIONS * (CHUNKS - EARLY) * PER_CHUNK)

        @block.gpsimd
        def _(pool):
            nc.gpsimd.iota(log_table[:], pattern=[[1, TABLE]], base=-(W - 1), channel_multiplier=0,
                           allow_small_or_imprecise_dtypes=True).then_inc(indices_made, 1)
            pool.wait_ge(indices_made, 1)
            for q in range(SLOTS):
                nc.gpsimd.iota(slot_col[HID * q:HID * (q + 1), :], pattern=[[1, 1]], base=W * q,
                               channel_multiplier=0, allow_small_or_imprecise_dtypes=True).then_inc(indices_made, 1)
            pool.wait_ge(indices_made, SLOTS + 1)
            nc.gpsimd.memset(ident[:], 0.0).then_inc(ident_made, 1)
            pool.wait_ge(ident_made, 1)
            nc.gpsimd.affine_select(out=ident[:], in_=ident[:], compare_op=ALU.not_equal, fill=1.0, base=0,
                                    pattern=[[-1, P]], channel_multiplier=1).then_inc(ident_made, 1)
            pool.wait_ge(ident_made, 2)
            nc.gpsimd.memset(mats[:, 1].rearrange("p n e -> p (n e)"), 0.0).then_inc(mats_zeroed, 1)
            pool.wait_ge(tables_made, 1)
            pool.wait_ge(logs_made, 2)

            def stage(k, mix_a, groups):
                if not groups:
                    return
                for cc in range(CHUNKS):
                    if mix_a and cc == 0:
                        pool.wait_ge(tables_made, 2)

                    def pair(p):
                        for half in range(2):
                            T = p * 2 + (2 * PAIRS * cc + half)
                            for g in range(groups):
                                if nd_by_dve(cc, half, g, groups):
                                    continue
                                wait_hidden_free(pool, k, cc, T, g, groups)
                                make_nd(pool, hidden_tile(cc, p, half, g, groups), k * W + T * ROWS, g)\
                                    .then_inc(nd_ready, 1)
                    each_pair(pool, pair, unrolled=(not mix_a and cc == 0))

            stages(pool, stage)

        @block.scalar
        def _(act):
            act.wait_ge(zeroed, 1)
            nc.scalar.activation(relu_b1[:], zero_col[:], ACT.Ln, bias=1.0).then_inc(table_loaded, 1)
            nc.scalar.activation(mats[:, 0].rearrange("p n e -> p (n e)"), zero_col[:].to_broadcast([P, P * CHUNK]),
                                 ACT.Copy).then_inc(mats_zeroed, 1)
            act.wait_ge(logs_wanted, 1)
            nc.scalar.activation(row_scale[:, 0:W], row_scale[:, 0:W], ACT.Ln, bias=1.0, scale=c_col[:, 0:1])\
                .then_inc(logs_made, 1)
            act.wait_ge(logs_wanted, 2)
            nc.scalar.activation(log_table[:], log_table[:], ACT.Ln, bias=1.0, scale=c_col[:, 0:1]).then_inc(logs_made, 1)
            nc.scalar.activation(row_scale[:, W:], row_scale[:, W:], ACT.Ln, bias=1.0, scale=c_col[:, 0:1])\
                .then_inc(logs_made, 1)
            act.wait_ge(w1_in, 2 * DMA)
            act.wait_ge(table_loaded, 1)
            nc.scalar.activation(relu_b1[:], b1_col[:], ACT.Relu).then_inc(relu_b1_made, 1)

            def add_const_bias(k, mix_a, cc):
                act.wait_ge(x_in[cc], k * PER_CHUNK + PER_CHUNK)
                if mix_a:
                    act.wait_ge(main_ready, tiles_before(a_chunk(k - 1, cc) + 1))
                chunk = y[high_half, cc * CHUNK:(cc + 1) * CHUNK, :]
                x_chunk = x_last[high_half] if cc == CHUNKS - 1 else chunk
                nc.scalar.activation(chunk, x_chunk, ACT.Identity, bias=b2_col[high_half, 1:2]).then_inc(y_const_ready, 1)

            def stage(k, mix_a, groups):
                if not groups:
                    return
                for cc in range(CHUNKS):
                    def pair(p):
                        for half in range(2):
                            T = p * 2 + (2 * PAIRS * cc + half)
                            for g in range(groups):
                                made = nd_index(k, cc, p, half, g, groups)
                                act.wait_ge(nd_dve_ready if nd_by_dve(cc, half, g, groups) else nd_ready, made + 1)
                                tile = hidden_tile(cc, p, half, g, groups)
                                nc.scalar.activation(tile, tile, ACT.Relu, bias=b1_col[:, 0:1],
                                                     scale=w1_col[:, 0:1]).then_inc(hidden_ready, 1)
                    if groups == 2:
                        each_pair(act, pair)
                    else:
                        for p in range(PAIRS):
                            pair(p)
                            at_once = (0, CHUNKS - 1) if not mix_a else (CHUNKS - 1,)
                            if p == 0 and cc > 0 and cc - 1 not in at_once:
                                add_const_bias(k, mix_a, cc - 1)
                            if p == PAIRS - 1 and cc in at_once:
                                if cc == 0:
                                    act.wait_ge(const_bias_read, 1)
                                add_const_bias(k, mix_a, cc)
                if mix_a:
                    act.wait_ge(early_out, k * (EARLY * PER_CHUNK))
                    act.wait_ge(late_out, k * ((CHUNKS - EARLY) * PER_CHUNK))
                else:
                    act.wait_ge(b_mats_out, 2 * DMA)
                with act.Fori(0, TILES // 2) as p:
                    for half in range(2):
                        T = p * 2 + half
                        act.wait_ge(main_ready, b_tile(k, T) + 1)
                        nc.scalar.activation(mixed[:, :, bass.ds(T * ROWS, ROWS)],
                                             slot_of(main, half).rearrange("p (s t) -> p t s", s=ROWS),
                                             ACT.Copy).then_inc(main_taken, 1)

            stages(act, stage)

        @block.vector
        def _(dve):
            steps = [0]

            def step(instruction):
                steps[0] += 1
                instruction.then_inc(dve_step, 1)
                dve.wait_ge(dve_step, steps[0])

            def absolute(ap):
                return dve.scalar_tensor_tensor(out=ap, in0=ap, scalar=-1.0, in1=ap, op0=ALU.mult, op1=ALU.max)

            dve.memset(zero_col[:], 0.0).then_inc(zeroed, 1)
            dve.memset(w2_blocks[:], 0.0).then_inc(zeroed, 1)
            dve.wait_ge(consts_in, 3 * DMA)
            step(absolute(c_col[:]))
            step(dve.tensor_tensor(thr_col[:, 2:3], thr_col[:, 0:1], thr_col[:, 1:2], ALU.mult))
            step(absolute(thr_col[:, 2:3]))
            dve.wait_ge(indices_made, SLOTS + 1)
            dve.tensor_scalar(row_scale[:, 0:W], log_table[:, W - 1:2 * W - 1], thr_col[:, 2:3], None, ALU.max)\
               .then_inc(logs_wanted, 1)
            step(dve.tensor_scalar(row_scale[:, W:], log_table[:, 2 * W - 1:], thr_col[:, 2:3], None, ALU.max))
            dve.tensor_scalar(log_table[:], log_table[:], slot_col[:, 0:1], 0.0, ALU.subtract, ALU.max)\
               .then_inc(logs_wanted, 1)

            def square(ap):
                return ap.rearrange("p (b m n) -> p b m n", b=BLOCKS, m=H)

            def rank_one(part, i, dst):
                shape = [P, BLOCKS, H, H]
                u = first[part].rearrange("p (b i m) -> p b i m", b=BLOCKS, i=2)[:, :, i, :]
                v = second[part].rearrange("p (b i m) -> p b i m", b=BLOCKS, i=2)[:, :, i, :]
                return dve.tensor_tensor(square(dst), u.unsqueeze(3).to_broadcast(shape),
                                         v.unsqueeze(2).to_broadcast(shape), ALU.mult)

            def diagonal(ap, blocks):
                return bass.AP(ap.tensor, ap.offset, [list(ap.ap[0]), [H * H, blocks], [H + 1, H]])

            def compact(part):
                dve.wait_ge(weights_in[part], DMA * (3 + (part == "a")))
                if part == "a":
                    eye = diagonal(w_eye, 1)
                    step(dve.tensor_scalar(eye, eye, 1.0, None, ALU.add))
                rank_one(part, 0, comp[part])
                step(rank_one(part, 1, term[part]))
                step(dve.tensor_tensor(comp[part], comp[part], term[part], ALU.add))
                if part == "a":
                    whole = comp[part].rearrange("p (b f) -> p b f", b=BLOCKS)
                    step(dve.tensor_tensor(whole, whole, w_eye.unsqueeze(1).to_broadcast([P, BLOCKS, H * H]), ALU.add))
                on = diagonal(comp[part], BLOCKS)
                dve.tensor_tensor(on, on, diag[part].rearrange("p (b m) -> p b m", b=BLOCKS), ALU.add)\
                   .then_inc(comp_made, 1)

            def invert(part):
                step(dve.tensor_scalar(row_scale[:, part], row_scale[:, part], EPS, None, ALU.add))
                dve.reciprocal(row_scale[:, part], row_scale[:, part]).then_inc(tables_made, 1)

            dve.wait_ge(logs_made, 1)
            invert(slice(0, W))
            dve.wait_ge(b2_in, DMA)
            step(dve.tensor_copy(b2_col[:, 1:2], b2_col[:, 0:1]))
            dve.wait_ge(const_bias_made, 1)
            dve.tensor_tensor(b2_col[P // 2:, 1:2], b2_col[P // 2:, 0:1], bias[P // 2:, 1, 0:1], ALU.add)\
               .then_inc(const_bias_read, 1)
            dve.wait_ge(const_bias_read, 1)

            compact("b")

            def finish_tile(k, T, half):
                dve.wait_ge(main_taken, b_tile(k, TILES - 1) + 1)
                dve.wait_ge(main_ready, a_tile(k, T) + 1)
                dve.tensor_tensor(rows(mixed, T * ROWS, ROWS), slot_of(main, half), rows(mixed, T * ROWS, ROWS),
                                  ALU.add).then_inc(main_taken, 1)

            def falling(half, first_col, first_partition, partitions, n_rows):
                return bass.AP(bias, first_partition * 2 * COLS + half * COLS + first_col + W - 1,
                               [[2 * COLS, partitions], [W, n_rows], [-1, W]])

            def add_bias(k, cc, T, half, groups):
                dve.wait_ge(x_in[cc], k * PER_CHUNK + PER_CHUNK)
                x_of, first = (x_last, T * ROWS - cc * CHUNK) if cc == CHUNKS - 1 else (y, T * ROWS)
                last = T == TILES - 1
                for n in range(2 if last or groups == 1 else 1):
                    if last and n == 0:
                        dve.wait_ge(first_bank_ready, k + 1)
                    else:
                        dve.wait_ge(hidden_used, hidden_index(k, T, groups - 1, groups) + 1)
                    top = n * (ROWS // 2)
                    n_rows = ROWS // 2 if last or groups == 1 else ROWS
                    into, from_partition = (slice(0, P), 0) if groups == 2 else (low_half, n * (P // 2))
                    add = dve.scalar_tensor_tensor(
                        out=y[into, T * ROWS + top:T * ROWS + top + n_rows, :],
                        in0=falling(half, n * BANK, from_partition, into.stop, n_rows), scalar=b2_col[into, 0:1],
                        in1=x_of[into, first + top:first + top + n_rows, :], op0=ALU.add, op1=ALU.add)
                add.then_inc(y_ready, 1)

            def stage(k, mix_a, groups):
                to_add = []
                for a, biases in stage_steps(mix_a, groups) + [(None, [])]:
                    for T in biases:
                        U = T + 1
                        cc, p = U // (2 * PAIRS), U % (2 * PAIRS) // 2
                        if U < TILES and nd_by_dve(cc, U % 2, 1, groups):
                            wait_hidden_free(dve, k, cc, U, 1, groups)
                            make_nd(dve, hidden_tile(cc, p, U % 2, 1, groups), k * W + U * ROWS, 1)\
                                .then_inc(nd_dve_ready, 1)
                    if a is not None:
                        finish_tile(k - 1, a, a % 2)
                    for T in to_add:
                        add_bias(k, T // (2 * PAIRS), T, T % 2, groups)
                    to_add = biases
                    if not mix_a and 1 in biases:
                        for half in range(2):
                            dve.wait_ge(main_ready, half + 1)
                            dve.tensor_copy(turned["b"][:, half * COLS:(half + 1) * COLS], slot_of(main, half))\
                               .then_inc(main_taken, 1)
                if not mix_a:
                    dve.wait_ge(y_const_ready, CHUNKS)
                    compact("a")
                    dve.wait_ge(logs_made, 3)
                    invert(slice(W, S))
                    for half in range(2):
                        dve.wait_ge(a_transposed, half + 1)
                        dve.tensor_copy(turned["a"][:, half * COLS:(half + 1) * COLS], slot_of(bias, half))\
                           .then_inc(a_turned, 1)

            stages(dve, stage)

        @block.tensor
        def _(pe):
            def transposes(part, psum, ready):
                pe.wait_ge(comp_made, 1 + (part == "a"))
                for half in range(2):
                    for b in range(BLOCKS):
                        at = (2 * b + half) * P
                        mm = pe.transpose(psum[:, half, b * P:(b + 1) * P], comp[part][:, at:at + P], ident[:])
                    mm.then_inc(ready, 1)

            pe.wait_ge(ident_made, 2)
            pe.wait_ge(w2_in, SLOTS * DMA)
            pe.wait_ge(relu_b1_made, 1)
            for g in range(2):
                mm = pe.matmul(bias[:, 1, 0:1], w2_blocks[:, g, :], relu_b1[:, 0:1], start=(g == 0), stop=(g == 1))
            mm.then_inc(const_bias_made, 1)
            pe.wait_ge(const_bias_read, 1)

            def a_rows(k, cc, T, half, first_row):
                pe.wait_ge(main_taken, a_tile(k, T) - 1)
                for j in range(ROWS):
                    mm = pe.matmul(main[:, half, j * W:(j + 1) * W],
                                   mats[:, cc % 2, :, first_row + j], y[:, T * ROWS + j, :], start=True, stop=True)
                mm.then_inc(main_ready, 1)

            def bias_tile(k, T, groups):
                half, p = T % 2, T % (2 * PAIRS) // 2
                wait(pe, y_ready, region_tiles(k, T) - 1)
                pe.wait_ge(hidden_ready, hidden_index(k, T, groups - 1, groups) + 1)
                for at in range(0, COLS, BANK):
                    for g in range(groups):
                        into = low_half if (g if groups == 2 else at // BANK) == 0 else high_half
                        mm = pe.matmul(bias[into, half, at:at + BANK], w2_blocks[:, g, P // 2 * g:P // 2 * (g + 1)],
                                       hidden_tile(T // (2 * PAIRS), p, half, g, groups)[:, at:at + BANK],
                                       start=True, stop=True)
                        if at == COLS - BANK:
                            mm.then_inc(hidden_used, 1)
                        elif T == TILES - 1 and g == groups - 1:
                            mm.then_inc(first_bank_ready, 1)

            def stage(k, mix_a, groups):
                for a, biases in stage_steps(mix_a, groups):
                    if a is not None:
                        cc = a // (2 * PAIRS)
                        if a % (2 * PAIRS) == 0:
                            pe.wait_ge(mats_in[cc % 2], ring_use(a_chunk, k - 1, cc) * PER_CHUNK)
                        a_rows(k - 1, cc, a, a % 2, a * ROWS - cc * CHUNK)
                    for T in biases:
                        if not mix_a and T == 1:
                            transposes("b", main, main_ready)
                        bias_tile(k, T, groups)
                if not groups:
                    return
                pe.wait_ge(y_ready, region_tiles(k, TILES))
                if groups == 1:
                    pe.wait_ge(y_const_ready, k * CHUNKS + CHUNKS)
                for cc in range(CHUNKS):
                    pe.wait_ge(mats_in[cc % 2], ring_use(b_chunk, k, cc) * PER_CHUNK)

                    def columns(p):
                        for half in range(2):
                            T = p * 2 + (2 * PAIRS * cc + half)
                            pe.wait_ge(main_taken, b_tile(k, T) - 1)
                            for j in range(ROWS):
                                at = p * (2 * ROWS) + (half * ROWS + j)
                                mm = pe.matmul(main[:, half, j * W:(j + 1) * W], mats[:, cc % 2, :, at],
                                               y[:, :, cc * CHUNK + at],
                                               start=True, stop=True)
                            mm.then_inc(main_ready, 1)
                    each_pair(pe, columns, unrolled=True)
                    if not mix_a and cc == 1:
                        transposes("a", bias, a_transposed)

            stages(pe, stage)


_INS = ["x", "L0_conv_W1", "L0_conv_b1", "L0_conv_W2", "L0_conv_b2", "L0_conv_c", "L0_conv_L_multiplier",
        "L0_conv_init_L", "L1_conv_qw1", "L1_conv_qw2", "L1_conv_kw1", "L1_conv_kw2", "L1_conv_qdd", "L1_conv_kdd",
        "L1_conv_w"]


def kernel(**inputs):
    import numpy as np
    import concourse.bacc as bacc
    from concourse.bass_utils import run_bass_kernel_spmd

    nc = bacc.Bacc("TRN2", target_bir_lowering=False, num_devices=1)
    arrays, args = {}, []
    for name in _INS:
        a = np.ascontiguousarray(inputs[name])
        if a.ndim < 2 and a.size == 1:
            a = a.reshape(1, 1)
        arrays[f"in_{name}"] = a
        args.append(nc.dram_tensor(f"in_{name}", a.shape, mybir.dt.from_np(a.dtype), kind="ExternalInput").ap())
    result = nc.dram_tensor("out_mixed", (1, H, S, S), F32, kind="ExternalOutput").ap()
    build(nc, *args, result)
    r = run_bass_kernel_spmd(nc, [arrays], core_ids=[0])
    return r.results[0]["out_mixed"]
```
